# Optimizing a Trainium2 kernel written in Bass

```python
import numpy as np
import jax
import jax.numpy as jnp

def _softmax(x, axis=-1):
    return jax.nn.softmax(x, axis=axis)

def _gelu(x):
    return jax.nn.gelu(x, approximate=True)

def _silu(x):
    return jax.nn.silu(x)

def _sigmoid(x):
    return jax.nn.sigmoid(x)

def _layernorm(x, axis=-1, eps=1e-05):
    m = jnp.mean(x, axis=axis, keepdims=True)
    v = jnp.var(x, axis=axis, keepdims=True)
    return (x - m) / jnp.sqrt(v + eps)

def _scatter_add(tgt, idx, src, axis=0):
    return tgt.at[idx].add(src)

def _segment_sum(src, seg, n):
    return jax.ops.segment_sum(src, seg, n)
kernel_name = 'mk_rec_standalone_d1_rec_r8_39cea7'

def setup_inputs(seed: int=0):
    np.random.seed(seed)
    _w = jnp.asarray

    def _rec_inputs():
        import jax
        import jax.numpy as jnp
        _rk = jax.random.key(seed)
        r_rate_idx = jax.random.randint(jax.random.fold_in(_rk, 1), (2048,), 0, 6, jnp.int32)
        r_genre_idx = jax.random.randint(jax.random.fold_in(_rk, 2), (2048, 25), 0, 2, jnp.int32)
        r_director_idx = jax.random.randint(jax.random.fold_in(_rk, 3), (2048, 2186), 0, 2, jnp.int32)
        r_actors_idx = jax.random.randint(jax.random.fold_in(_rk, 4), (2048, 8030), 0, 2, jnp.int32)
        return (r_rate_idx, r_genre_idx, r_director_idx, r_actors_idx)
    r_rate_idx, r_genre_idx, r_director_idx, r_actors_idx = _rec_inputs()

    def _L0_rec_setup():
        import jax, jax.numpy as jnp
        import numpy as np
        NUM_RATE, NUM_GENRE, NUM_DIRECTOR, NUM_ACTOR = (6, 25, 2186, 8030)
        EMB_DIM = 64
        B = 2048

        def _multihot_emb(idx_int, W):
            x = idx_int.astype(jnp.float32)
            emb = jnp.einsum('bv,ev->be', x, W)
            return emb / jnp.sum(x, axis=1, keepdims=True)
        key = jax.random.key(seed)
        ks = jax.random.split(key, 10)
        rate_idx = jax.random.randint(ks[0], (B,), 0, NUM_RATE)
        genre_idx = jax.random.randint(ks[1], (B, NUM_GENRE), 0, 2)
        director_idx = jax.random.randint(ks[2], (B, NUM_DIRECTOR), 0, 2)
        actors_idx = jax.random.randint(ks[3], (B, NUM_ACTOR), 0, 2)
        emb_rate = jax.random.normal(ks[4], (NUM_RATE, EMB_DIM), jnp.float32)
        W_genre = jax.random.normal(ks[5], (EMB_DIM, NUM_GENRE), jnp.float32) / np.sqrt(NUM_GENRE)
        W_director = jax.random.normal(ks[6], (EMB_DIM, NUM_DIRECTOR), jnp.float32) / np.sqrt(NUM_DIRECTOR)
        W_actor = jax.random.normal(ks[7], (EMB_DIM, NUM_ACTOR), jnp.float32) / np.sqrt(NUM_ACTOR)
        W_lin = jax.random.normal(ks[8], (EMB_DIM, 4 * EMB_DIM), jnp.float32) / np.sqrt(4 * EMB_DIM)
        b_lin = jax.random.normal(ks[9], (EMB_DIM,), jnp.float32) * 0.01
        return {'rate_idx': rate_idx, 'genre_idx': genre_idx, 'director_idx': director_idx, 'actors_idx': actors_idx, 'emb_rate': emb_rate, 'W_genre': W_genre, 'W_director': W_director, 'W_actor': W_actor, 'W_lin': W_lin, 'b_lin': b_lin}
    _L0_rec_all = _L0_rec_setup()
    _L0_rec_in = {k: v for k, v in _L0_rec_all.items() if k in ('emb_rate', 'W_genre', 'W_director', 'W_actor', 'W_lin', 'b_lin')}
    del _L0_rec_all
    return {'r_rate_idx': r_rate_idx, 'r_genre_idx': r_genre_idx, 'r_director_idx': r_director_idx, 'r_actors_idx': r_actors_idx, 'L0_rec_emb_rate': _L0_rec_in['emb_rate'], 'L0_rec_W_genre': _L0_rec_in['W_genre'], 'L0_rec_W_director': _L0_rec_in['W_director'], 'L0_rec_W_actor': _L0_rec_in['W_actor'], 'L0_rec_W_lin': _L0_rec_in['W_lin'], 'L0_rec_b_lin': _L0_rec_in['b_lin']}

def reference(r_rate_idx, r_genre_idx, r_director_idx, r_actors_idx, L0_rec_emb_rate, L0_rec_W_genre, L0_rec_W_director, L0_rec_W_actor, L0_rec_W_lin, L0_rec_b_lin):
    import jax
    import jax.numpy as jnp

    def _L0_rec_ref(rate_idx, genre_idx, director_idx, actors_idx, emb_rate, W_genre, W_director, W_actor, W_lin, b_lin):
        import jax, jax.numpy as jnp
        import numpy as np
        NUM_RATE, NUM_GENRE, NUM_DIRECTOR, NUM_ACTOR = (6, 25, 2186, 8030)
        EMB_DIM = 64
        B = 2048

        def _multihot_emb(idx_int, W):
            x = idx_int.astype(jnp.float32)
            emb = jnp.einsum('bv,ev->be', x, W)
            return emb / jnp.sum(x, axis=1, keepdims=True)
        rate_emb = emb_rate[rate_idx]
        genre_emb = _multihot_emb(genre_idx, W_genre)
        director_emb = _multihot_emb(director_idx, W_director)
        actors_emb = _multihot_emb(actors_idx, W_actor)
        feats = jnp.concatenate((rate_emb, genre_emb, director_emb, actors_emb), axis=1)
        return jnp.einsum('bf,ef->be', feats, W_lin) + b_lin
    y = _L0_rec_ref(r_rate_idx, r_genre_idx, r_director_idx, r_actors_idx, L0_rec_emb_rate, L0_rec_W_genre, L0_rec_W_director, L0_rec_W_actor, L0_rec_W_lin, L0_rec_b_lin)
    return y

_drawn_inputs = setup_inputs


def setup_inputs(seed=0):
    import zlib

    import numpy as np

    out = dict(_drawn_inputs(seed))
    spreads = {}
    factors = {'L0_rec_W_director': 64.0, 'L0_rec_W_actor': 200.0}
    for name, (base, spread) in spreads.items():
        noise = np.random.default_rng([zlib.crc32(name.encode()), seed]).standard_normal(out[name].shape)
        drawn = base * np.exp(spread * noise) if base else spread * noise
        out[name] = jnp.asarray(drawn.astype(out[name].dtype))
    for name, factor in factors.items():
        out[name] = (out[name] * factor).astype(out[name].dtype)
    return out
```

```python
from contextlib import ExitStack

import concourse.bass as bass
from concourse import mybir

ALU = mybir.AluOpType
ACT = mybir.ActivationFunctionType
AX_X = mybir.AxisListType.X
BF16 = mybir.dt.bfloat16
F32 = mybir.dt.float32
I32 = mybir.dt.int32
U32 = mybir.dt.uint32

P = 128
E = 64
RATES, GENRES, DIRECTORS, ACTORS = 6, 25, 2186, 8030
BATCH = 2048
NQ = 4
COLS = BATCH // NQ
TILES = COLS // P

DIR_CHUNKS = DIRECTORS // P
DIR_TAIL = DIRECTORS - DIR_CHUNKS * P
ACT_CHUNKS = ACTORS // P
ACT_TAIL = ACTORS - ACT_CHUNKS * P
GENRE_AT = 96
CHUNKS = DIR_CHUNKS + 1 + ACT_CHUNKS
SLAB = 8
HALF = SLAB // 2
SLABS = CHUNKS // SLAB
SHARED = DIR_CHUNKS
assert CHUNKS % SLAB == 0 and ACT_TAIL <= GENRE_AT and GENRE_AT + GENRES <= P and DIR_CHUNKS == 2 * SLAB + 1

W_GENRE, W_DIRTAIL, W_STREAM = 0, 1, 2
WSLOTS = W_STREAM + CHUNKS
W_FIRST = W_STREAM + DIR_CHUNKS
PIECE = 16
W_PIECES = [(0, 10), (10, W_FIRST)] + [(at, min(at + PIECE, WSLOTS)) for at in range(W_FIRST, WSLOTS, PIECE)]
XRING = 5
BRING = 2
assert SLABS % XRING == 0 and SLABS % BRING == 0
WORDS = HALF * COLS // 2
FORBIDDEN = 0xFFFFFFFF ^ 0x3F803F80
GEN, DIR, ACTR = 0, 1, 2


def rec_head(nc, x_stream, x_dirtail, rate, w_all, emb_rate_t, w_lin_t, bias, out):
    with ExitStack() as ctx:
        def sb(name, shape, dt):
            return ctx.enter_context(nc.sbuf_tensor(name, shape, dt))

        def bank(name):
            return ctx.enter_context(nc.psum_tensor(name, [P, COLS], F32))

        def sem(name):
            return ctx.enter_context(nc.semaphore(name))

        x_raw = sb("x_raw", [P, XRING, 2, HALF * COLS], I32)
        x_bf = sb("x_bf", [P, BRING, 2, HALF * COLS], BF16)
        w32 = sb("w32", [P, WSLOTS, E], F32)
        w_parts = sb("w_parts", [P, WSLOTS, 4, E], BF16)
        tail_raw = sb("tail_raw", [DIR_TAIL, COLS], I32)
        tail_bf = sb("tail_bf", [DIR_TAIL, COLS], BF16)
        rate_i = sb("rate_i", [RATES, COLS], I32)
        onehot = sb("onehot", [RATES + 1, COLS], F32)
        rate_wrap = sb("rate_wrap", [RATES, COLS], F32)
        row_no_i = sb("row_no_i", [RATES, 1], I32)
        row_no = sb("row_no", [RATES, 1], F32)
        emb_t = sb("emb_t", [E, RATES], F32)
        lin_rate = sb("lin_rate", [E, E], F32)
        lin_twice = sb("lin_twice", [P, 3, E], F32)
        lin_low = sb("lin_low", [P, 3, E + 1], F32)
        rate_table = sb("rate_table", [RATES + 1, E], F32)
        products = sb("products", [P, 2, 2, COLS], F32)
        him = products[:, 0]
        slo = products[:, 1]
        w_rest = products[:, :, :, :].rearrange("p a b n -> p a (b n)").rearrange("p a (s e) -> p a s e", e=E)
        inv = sb("inv", [P, TILES, 1], F32)
        term = sb("term", [P, TILES, E], F32)
        rate_terms = sb("rate_terms", [P, NQ, TILES, E], F32)
        out_sb = sb("out_sb", [P, TILES, E], F32)
        seen = sb("seen", [P, 2, WORDS], U32)
        worst = sb("worst", [P, 1], F32)
        wide_x = x_raw[:, 0, :, :].bitcast(F32)
        wide_tail = tail_raw[:, :].bitcast(F32)
        wide_w = x_raw[:, 1, :, :].bitcast(F32).rearrange("p h (s o e) -> p h s o e", o=2, e=E)
        wide_w_fixed = x_raw[:, 2, 0, 0:2 * 2 * E].bitcast(F32).rearrange("p (s o e) -> p s o e", o=2, e=E)
        ones_f = sb("ones_f", [P, 1], F32)
        wide = sb("wide", [1, 1], I32)

        dir_hm, dir_sl = bank("dir_hm"), bank("dir_sl")
        gen_hm, gen_sl = bank("gen_hm"), bank("gen_sl")
        act_hm, act_sl = bank("act_hm"), bank("act_sl")
        lin0, lin1 = bank("lin0"), bank("lin1")

        landed = [[sem(f"x_landed_{r}_{h}") for h in range(2)] for r in range(XRING)]
        w_landed = [sem(f"w_landed_{i}") for i in range(2)]
        tail_landed, rate_landed, small_landed = sem("tail_landed"), sem("rate_landed"), sem("small_landed")
        conv = [sem("conv_by_vector"), sem("conv_by_scalar")]
        checked = sem("checked")
        used = sem("slabs_used")
        hi_done, rest_done, mid_done, lo_done = sem("hi_done"), sem("rest_done"), sem("mid_done"), sem("lo_done")
        tail_conv, tail_seen = sem("tail_conv"), sem("tail_seen")
        zeroed = sem("zeroed")
        pool_step = sem("pool_step")
        rate_step, lin_low_set = sem("rate_step"), sem("lin_low_set")
        onehot_ready = sem("onehot_ready")
        table_mm, table_ready = sem("table_mm"), sem("table_ready")
        dir_mm, gen_mm = sem("dir_mm"), sem("gen_mm")
        copied = sem("products_copied")
        first_copied = sem("first_copied")
        inverted = sem("sums_inverted")
        lin_mm = sem("linear_mm")
        merged = sem("merged")
        term_ready = sem("term_ready")
        out_done, out_free = sem("out_done"), sem("out_free")
        or_step, verdict_mm, verdict = sem("or_step"), sem("verdict_mm"), sem("verdict")

        wide_landed = [sem(f"wide_landed_{h}") for h in range(2)]
        wide_conv = [sem(f"wide_converted_{h}") for h in range(2)]
        wide_used = [sem(f"wide_used_{h}") for h in range(2)]
        wide_tail_landed, wide_tail_conv = sem("wide_tail_landed"), sem("wide_tail_converted")
        wide_fixed, wide_staged = sem("wide_fixed"), sem("wide_staged")
        wide_copied, wide_lin = sem("wide_copied"), sem("wide_linear_mm")
        wide_step, wide_merged, wide_stored = sem("wide_step"), sem("wide_merged"), sem("wide_stored")
        wide_free = sem("wide_out_free")

        started = {"pe": [used, dir_mm, lin_mm, *wide_used], "act": [copied], "dve": [checked, tail_seen, merged], "pool": [out_free, wide_free]}

        def past(n):
            return n + 1

        block = ctx.enter_context(nc.Block())
        first_cols = W_FIRST * E

        @block.sync
        def _(sp):
            sp.dma_start(w32[:, 0:W_FIRST, :].rearrange("p s e -> p (s e)"), w_all[:, 0:first_cols]).then_inc(w_landed[0], 16)
            sp.dma_start(tail_raw[:, :], x_dirtail[:, 0:COLS]).then_inc(tail_landed, 16)
            sp.dma_start(rate_i[:, :], rate[:, 0:COLS].broadcast_to([RATES, COLS])).then_inc(rate_landed, 16)
            sp.dma_start(w32[:, W_FIRST:, :].rearrange("p s e -> p (s e)"), w_all[:, first_cols:]).then_inc(w_landed[1], 16)
            for r in range(XRING):
                for h in range(2):
                    sp.dma_start(x_raw[:, r, h, :], x_stream[r, h]).then_inc(landed[r][h], 16)

            def refill(q, s):
                for h in range(2):
                    sp.wait_ge(conv[h], q * SLABS + s + 1)
                    sp.dma_start(x_raw[:, s % XRING, h, :],
                                 x_stream[bass.ds(q * SLABS + s + XRING, 1), h].rearrange("s p n -> (s p) n")
                                 ).then_inc(landed[s % XRING][h], 16)

            def store(q):
                sp.wait_ge(merged, past(4 * q + 4))
                sp.dma_start(out[bass.ds(q * COLS, COLS), :].rearrange("(t p) e -> p t e", p=P), out_sb[:, :, :]
                             ).then_inc(out_done, 16)

            with sp.Fori(0, NQ - 1) as q:
                for s in range(SLABS):
                    if s == 4:
                        sp.wait_ge(tail_conv, q + 1)
                        sp.dma_start(tail_raw[:, :], x_dirtail[:, bass.ds((q + 1) * COLS, COLS)]).then_inc(tail_landed, 16)
                        sp.wait_ge(onehot_ready, q + 1)
                        sp.dma_start(rate_i[:, :], rate[:, bass.ds((q + 1) * COLS, COLS)].broadcast_to([RATES, COLS])
                                     ).then_inc(rate_landed, 16)
                    refill(q, s)
                store(q)
            for s in range(SLABS - XRING):
                refill(NQ - 1, s)
            store(NQ - 1)
            sp.wait_ge(out_done, 16 * NQ)

            sp.wait_ge(verdict, 1)
            with sp.If(sp.value_load(wide[0:1, 0:1], min_val=0, max_val=1) == 1):
                with sp.Fori(0, NQ) as q:
                    sp.dma_start(tail_raw[:, :], x_dirtail[:, bass.ds(q * COLS, COLS)]).then_inc(wide_tail_landed, 16)
                    with sp.Fori(0, SLABS) as s:
                        slab = sp.snap(q * SLABS + s)
                        for h in range(2):
                            sp.wait_ge(wide_used[h], past(slab))
                            sp.dma_start(x_raw[:, 0, h, :], x_stream[bass.ds(slab, 1), h].rearrange("s p n -> (s p) n")
                                         ).then_inc(wide_landed[h], 16)
                    row = sp.snap(q * COLS)
                    sp.wait_ge(wide_merged, 3 * q + 3)
                    sp.dma_start(out[bass.ds(row, COLS), :].rearrange("(t p) e -> p t e", p=P), out_sb[:, :, :]
                                 ).then_inc(wide_stored, 16)
                    sp.wait_ge(wide_stored, 16 * q + 16)
                    sp.sem_inc(wide_free, 1)

        @block.gpsimd
        def _(pool):
            for signal in started["pool"]:
                pool.sem_inc(signal, 1)
            nc.gpsimd.memset(lin_low[:, :, :], 0.0).then_inc(pool_step, 1)
            pool.wait_ge(pool_step, 1)
            nc.gpsimd.memset(lin_low[0:1, :, E:E + 1], 1.0).then_inc(lin_low_set, 1)
            pool.wait_ge(lin_low_set, 1)
            nc.gpsimd.memset(w_parts[:, :, 2, :], 1.0).then_inc(pool_step, 1)
            pool.wait_ge(pool_step, 2)
            nc.gpsimd.memset(w_parts[GENRE_AT:P, W_STREAM + SHARED, 2, :], 0.0).then_inc(pool_step, 1)
            pool.wait_ge(pool_step, 3)
            for start in range(0, GENRE_AT, 32):
                nc.gpsimd.memset(w_parts[start:start + 32, W_GENRE, 2, :], 0.0).then_inc(pool_step, 1)
                pool.wait_ge(pool_step, 4 + start // 32)
            nc.gpsimd.memset(ones_f[:, :], 1.0).then_inc(pool_step, 1)
            pool.wait_ge(pool_step, 7)
            nc.gpsimd.memset(onehot[:, :], 1.0).then_inc(pool_step, 1)
            pool.wait_ge(pool_step, 8)
            nc.gpsimd.iota(row_no_i[:, :], [[0, 1]], base=0, channel_multiplier=1).then_inc(pool_step, 1)
            pool.wait_ge(pool_step, 9)
            nc.gpsimd.tensor_copy(row_no[:, :], row_no_i[:, :]).then_inc(pool_step, 1)
            pool.wait_ge(pool_step, 10)
            for q in range(NQ):
                pool.wait_ge(rate_landed, 16 * q + 16)
                if q >= 1:
                    pool.wait_ge(lin_mm, past(4 * q))
                nc.gpsimd.tensor_copy(onehot[0:RATES, :], rate_i[:, :]).then_inc(rate_step, 1)
                pool.wait_ge(rate_step, 4 * q + 1)
                nc.gpsimd.tensor_scalar(rate_wrap[:, :], onehot[0:RATES, :], 0.0, float(RATES), ALU.is_lt, ALU.mult).then_inc(rate_step, 1)
                pool.wait_ge(rate_step, 4 * q + 2)
                nc.gpsimd.tensor_tensor(onehot[0:RATES, :], onehot[0:RATES, :], rate_wrap[:, :], ALU.add).then_inc(rate_step, 1)
                pool.wait_ge(rate_step, 4 * q + 3)
                nc.gpsimd.tensor_scalar(rate_wrap[:, :], onehot[0:RATES, :], 0.0, float(RATES - 1), ALU.max, ALU.min).then_inc(rate_step, 1)
                pool.wait_ge(rate_step, 4 * q + 4)
                nc.gpsimd.tensor_scalar(onehot[0:RATES, :], rate_wrap[:, :], row_no[:, 0:1], None, ALU.is_equal).then_inc(onehot_ready, 1)
                if q >= 1:
                    pool.wait_ge(out_done, 16 * q)
                    pool.sem_inc(out_free, 1)

        def group_copy(bank_hm, bank_sl, slot):
            nc.scalar.copy(slo[:, slot, :], bank_sl[:, :]).then_inc(first_copied, 1)
            nc.scalar.copy(him[:, slot, :], bank_hm[:, :]).then_inc(copied, 1)

        @block.scalar
        def _(act):
            for signal in started["act"]:
                act.sem_inc(signal, 1)
            small = [(emb_t[:, :], emb_rate_t), (lin_rate[:, :], w_lin_t[0:E, :]), (rate_table[RATES:, :], bias)]
            for g in range(3):
                rows = w_lin_t[(g + 1) * E:(g + 2) * E, :]
                small += [(lin_twice[0:E, g, :], rows), (lin_twice[E:P, g, :], rows), (lin_low[E:P, g, 0:E], rows)]
            act.wait_ge(lin_low_set, 1)
            for dst, src in small:
                act.dma_start(dst, src).then_inc(small_landed, 16)
            def piece_mid(i):
                lo, hi = W_PIECES[i]
                act.wait_ge(rest_done, i + 1)
                nc.scalar.copy(w_parts[:, lo:hi, 1, :], w_rest[:, i % 2, 0:hi - lo, :]).then_inc(mid_done, 1)

            for i, (lo, hi) in enumerate(W_PIECES):
                act.wait_ge(w_landed[int(lo >= W_FIRST)], 16)
                nc.scalar.copy(w_parts[:, lo:hi, 0, :], w32[:, lo:hi, :]).then_inc(hi_done, 1)
                if i >= 1:
                    piece_mid(i - 1)
            piece_mid(len(W_PIECES) - 1)

            with act.Fori(0, NQ) as q:
                act.wait_ge(tail_landed, 16 * q + 16)
                act.wait_ge(dir_mm, past(q))
                act.wait_ge(tail_seen, past(q))
                nc.scalar.copy(tail_bf[:, :], tail_raw[:, :]).then_inc(tail_conv, 1)
                for s in range(SLABS):
                    act.wait_ge(landed[s % XRING][1], (q * (SLABS // XRING) + s // XRING + 1) * 16)
                    if s >= BRING:
                        act.wait_ge(used, past(q * SLABS + s - BRING + 1))
                        act.wait_ge(checked, past(q * SLABS + s - BRING + 1))
                    else:
                        act.wait_ge(used, past(q * SLABS))
                        act.wait_ge(checked, past(q * SLABS))
                    nc.scalar.copy(x_bf[:, s % BRING, 1, :], x_raw[:, s % XRING, 1, :]).then_inc(conv[1], 1)
                    if s == 4:
                        act.wait_ge(dir_mm, past(q + 1))
                        act.wait_ge(lin_mm, past(4 * q))
                        group_copy(dir_hm, dir_sl, 0)
                        act.wait_ge(gen_mm, q + 1)
                        group_copy(gen_hm, gen_sl, 1)
                act.wait_ge(used, past((q + 1) * SLABS))
                act.wait_ge(lin_mm, past(4 * q + 2))
                group_copy(act_hm, act_sl, 0)

            act.wait_ge(verdict, 1)
            with act.If(act.value_load(wide[0:1, 0:1], min_val=0, max_val=1) == 1):
                with act.Fori(0, NQ) as q:
                    act.wait_ge(wide_used[1], past(q * SLABS + SLABS))
                    nc.scalar.copy(slo[:, 0, :], dir_sl[:, :]).then_inc(wide_copied, 1)
                    nc.scalar.copy(slo[:, 1, :], gen_sl[:, :]).then_inc(wide_copied, 1)
                    nc.scalar.copy(him[:, 0, :], act_sl[:, :]).then_inc(wide_copied, 1)

        @block.vector
        def _(dve):
            for signal in started["dve"]:
                dve.sem_inc(signal, 1)
            nc.vector.memset(seen[:, :, :], 0).then_inc(zeroed, 1)

            def piece_lo(i):
                lo, hi = W_PIECES[i]
                dve.wait_ge(mid_done, i + 1)
                nc.vector.tensor_tensor(w_parts[:, lo:hi, 3, :], w_rest[:, i % 2, 0:hi - lo, :], w_parts[:, lo:hi, 1, :],
                                        ALU.subtract).then_inc(lo_done, 1)

            for i, (lo, hi) in enumerate(W_PIECES):
                dve.wait_ge(hi_done, i + 1)
                if i >= 2:
                    dve.wait_ge(lo_done, i - 1)
                nc.vector.tensor_tensor(w_rest[:, i % 2, 0:hi - lo, :], w32[:, lo:hi, :], w_parts[:, lo:hi, 0, :],
                                        ALU.subtract).then_inc(rest_done, 1)
                if i >= 1:
                    piece_lo(i - 1)
            piece_lo(len(W_PIECES) - 1)
            dve.wait_ge(zeroed, 1)
            dve.wait_ge(table_mm, 1)
            nc.vector.tensor_copy(rate_table[0:RATES, :], lin0[0:RATES, 0:E]).then_inc(table_ready, 1)

            def add_term(q, order, bank_lin):
                so_far = out_sb[:, :, :] if order > 1 else rate_terms[:, bass.ds(q, 1)].rearrange("p q t e -> p (q t) e")
                lin = bank_lin[:, 0:TILES * (E + 1)].rearrange("p (t e) -> p t e", t=TILES)
                dve.wait_ge(lin_mm, past(4 * q + order + 1))
                nc.vector.reciprocal(inv[:, :, :], lin[:, :, E:E + 1]).then_inc(inverted, 1)
                dve.wait_ge(inverted, 3 * q + order)
                nc.vector.tensor_tensor(term[:, :, :], lin[:, :, 0:E], inv[:, :, :].broadcast_to([P, TILES, E]),
                                        ALU.mult).then_inc(term_ready, 1)
                dve.wait_ge(term_ready, 3 * q + order)
                dve.wait_ge(merged, past(4 * q + order))
                nc.vector.tensor_tensor(out_sb[:, :, :], so_far, term[:, :, :], ALU.add).then_inc(merged, 1)

            with dve.Fori(0, NQ) as q:
                dve.wait_ge(tail_conv, q + 1)
                dve.wait_ge(checked, past(q * SLABS))
                tail_seen_words = seen[0:DIR_TAIL, 0, 0:COLS // 2]
                nc.vector.tensor_tensor(tail_seen_words, tail_seen_words, tail_bf[:, :].bitcast(U32),
                                        ALU.bitwise_or).then_inc(tail_seen, 1)
                dve.wait_ge(tail_seen, past(q + 1))
                for s in range(SLABS):
                    dve.wait_ge(landed[s % XRING][0], (q * (SLABS // XRING) + s // XRING + 1) * 16)
                    if s >= BRING:
                        dve.wait_ge(used, past(q * SLABS + s - BRING + 1))
                    else:
                        dve.wait_ge(used, past(q * SLABS))
                    dve.wait_ge(checked, past(q * SLABS + s))
                    nc.vector.tensor_copy(x_bf[:, s % BRING, 0, :], x_raw[:, s % XRING, 0, :]).then_inc(conv[0], 1)
                    dve.wait_ge(conv[0], q * SLABS + s + 1)
                    nc.vector.tensor_tensor(seen[:, 0, :], seen[:, 0, :], x_bf[:, s % BRING, 0, :].bitcast(U32), ALU.bitwise_or)
                    dve.wait_ge(conv[1], q * SLABS + s + 1)
                    nc.vector.tensor_tensor(seen[:, 1, :], seen[:, 1, :], x_bf[:, s % BRING, 1, :].bitcast(U32),
                                            ALU.bitwise_or).then_inc(checked, 1)
                    if s == 6:
                        dve.wait_ge(lin_mm, past(4 * q + 1))
                        rate_term = lin1[:, 0:TILES * (E + 1)].rearrange("p (t e) -> p t e", t=TILES)[:, :, 0:E]
                        nc.vector.tensor_copy(rate_terms[:, bass.ds(q, 1)].rearrange("p q t e -> p (q t) e"), rate_term
                                              ).then_inc(merged, 1)
                        dve.wait_ge(out_free, past(q))
                        add_term(q, 1, lin0)
                    if s == 7:
                        add_term(q, 2, lin1)
                add_term(q, 3, lin0)

            dve.wait_ge(checked, past(NQ * SLABS))
            nc.vector.tensor_tensor(seen[:, 0, :], seen[:, 0, :], seen[:, 1, :], ALU.bitwise_or).then_inc(or_step, 1)
            dve.wait_ge(or_step, 1)
            nc.vector.tensor_scalar(seen[:, 1, :], seen[:, 0, :], FORBIDDEN, None, ALU.bitwise_and).then_inc(or_step, 1)
            dve.wait_ge(or_step, 2)
            nc.vector.tensor_reduce(worst[:, :], seen[:, 1, :], AX_X, ALU.max).then_inc(or_step, 1)
            dve.wait_ge(verdict_mm, 1)
            nc.vector.tensor_scalar(wide[:, :], lin1[0:1, 0:1], 0.0, None, ALU.is_gt).then_inc(verdict, 1)

            dve.wait_ge(verdict, 1)
            with dve.If(dve.value_load(wide[0:1, 0:1], min_val=0, max_val=1) == 1):
                nc.vector.tensor_copy(wide_w_fixed[:, :, 0, :], w_parts[:, 0:2, 2, :]).then_inc(wide_fixed, 1)
                nc.vector.tensor_copy(wide_w_fixed[:, :, 1, :], w32[:, 0:2, :]).then_inc(wide_fixed, 1)
                with dve.Fori(0, NQ) as q:
                    dve.wait_ge(wide_tail_landed, 16 * q + 16)
                    nc.vector.tensor_copy(wide_tail, tail_raw[:, :]).then_inc(wide_tail_conv, 1)
                    with dve.Fori(0, SLABS) as s:
                        for h in range(2):
                            slots = bass.ds(s * SLAB + h * HALF + W_STREAM, HALF)
                            dve.wait_ge(wide_landed[h], (q * SLABS + s) * 16 + 16)
                            nc.vector.tensor_copy(wide_w[:, h, 0:HALF, 0, :], w_parts[:, slots, 2, :]).then_inc(wide_staged, 1)
                            nc.vector.tensor_copy(wide_w[:, h, 0:HALF, 1, :], w32[:, slots, :]).then_inc(wide_staged, 1)
                            nc.vector.tensor_copy(wide_x[:, h, :], x_raw[:, 0, h, :]).then_inc(wide_conv[h], 1)
                    dve.wait_ge(wide_free, past(q))
                    for g, bank_lin in enumerate((dir_hm, gen_hm, act_hm)):
                        lin = bank_lin[:, 0:TILES * (E + 1)].rearrange("p (t e) -> p t e", t=TILES)
                        so_far = out_sb[:, :, :] if g else rate_terms[:, bass.ds(q, 1)].rearrange("p q t e -> p (q t) e")
                        dve.wait_ge(wide_lin, 3 * q + g + 1)
                        nc.vector.reciprocal(inv[:, :, :], lin[:, :, E:E + 1]).then_inc(wide_step, 1)
                        dve.wait_ge(wide_step, 6 * q + 2 * g + 1)
                        nc.vector.tensor_tensor(term[:, :, :], lin[:, :, 0:E], inv[:, :, :].broadcast_to([P, TILES, E]),
                                                ALU.mult).then_inc(wide_step, 1)
                        dve.wait_ge(wide_step, 6 * q + 2 * g + 2)
                        nc.vector.tensor_tensor(out_sb[:, :, :], so_far, term[:, :, :], ALU.add).then_inc(wide_merged, 1)
                        dve.wait_ge(wide_merged, 3 * q + g + 1)

        @block.tensor
        def _(pe):
            for signal in started["pe"]:
                pe.sem_inc(signal, 1)
            def group_mm(slot, rhs, bank_hm, bank_sl, start, rows=P):
                nc.tensor.matmul(bank_hm[:, :], w_parts[0:rows, slot, 0:2, :].rearrange("p a e -> p (a e)"), rhs,
                                 start=start, stop=False, skip_group_check=True)
                return nc.tensor.matmul(bank_sl[:, :], w_parts[0:rows, slot, 2:4, :].rearrange("p a e -> p (a e)"), rhs,
                                        start=start, stop=False, skip_group_check=True)

            def chunk(s, j):
                return x_bf[:, bass.ds(s % BRING, 1), j // HALF, (j % HALF) * COLS:(j % HALF + 1) * COLS].rearrange("p s n -> p (s n)")

            def slot_mm(s, j, banks, start=False):
                hm, sl = banks
                w_hm = w_parts[:, bass.ds(s * SLAB + j + W_STREAM, 1), 0:2, :].rearrange("p s a e -> p (s a e)")
                w_sl = w_parts[:, bass.ds(s * SLAB + j + W_STREAM, 1), 2:4, :].rearrange("p s a e -> p (s a e)")
                nc.tensor.matmul(hm[:, :], w_hm, chunk(s, j), start=start, stop=False, skip_group_check=True)
                return nc.tensor.matmul(sl[:, :], w_sl, chunk(s, j), start=start, stop=False, skip_group_check=True)

            def slab_mm(q, s, banks, first=False):
                for j in range(SLAB):
                    if j % HALF == 0:
                        pe.wait_ge(conv[j // HALF], q * SLABS + s + 1)
                    last = slot_mm(s, j, banks, first and j == 0)
                last.then_inc(used, 1)
                return last

            def linear(g, bank_lin, slot):
                for t in range(TILES):
                    at = t * (E + 1)
                    cols = slice(t * P, (t + 1) * P)
                    nc.tensor.matmul(bank_lin[:, at:at + E + 1], slo[:, slot, cols], lin_low[:, g, :],
                                     start=True, stop=False, skip_group_check=True)
                    last = nc.tensor.matmul(bank_lin[:, at:at + E], him[:, slot, cols], lin_twice[:, g, :],
                                            start=False, stop=True, skip_group_check=True)
                last.then_inc(lin_mm, 1)

            pe.wait_ge(small_landed, 16 * 12)
            nc.tensor.matmul(lin0[0:RATES, 0:E], emb_t[:, :], lin_rate[:, :], start=True, stop=True).then_inc(table_mm, 1)
            pe.wait_ge(pool_step, 8)
            pe.wait_ge(lo_done, len(W_PIECES))
            pe.wait_ge(mid_done, len(W_PIECES))
            pe.wait_ge(hi_done, len(W_PIECES))
            pe.wait_ge(table_ready, 1)
            director, actor, genre = (dir_hm, dir_sl), (act_hm, act_sl), (gen_hm, gen_sl)
            with pe.Fori(0, NQ) as q:
                pe.wait_ge(tail_conv, q + 1)
                group_mm(W_DIRTAIL, tail_bf[:, :], *director, True, DIR_TAIL)
                with pe.Fori(0, 2) as s:
                    slab_mm(q, s, director)
                pe.wait_ge(conv[0], q * SLABS + 3)
                slot_mm(2, 0, director).then_inc(dir_mm, 1)
                group_mm(W_GENRE, chunk(2, 1), *genre, True).then_inc(gen_mm, 1)
                pe.wait_ge(copied, past(3 * q))
                slot_mm(2, 1, actor, True)
                for j in range(2, SLAB):
                    if j == HALF:
                        pe.wait_ge(conv[1], q * SLABS + 3)
                    last = slot_mm(2, j, actor)
                last.then_inc(used, 1)
                with pe.Fori(3, 6) as s:
                    slab_mm(q, s, actor)
                pe.wait_ge(merged, past(4 * q))
                pe.wait_ge(onehot_ready, q + 1)
                for t in range(TILES):
                    last = nc.tensor.matmul(lin1[:, t * (E + 1):t * (E + 1) + E], onehot[:, t * P:(t + 1) * P],
                                            rate_table[:, :], start=True, stop=True)
                last.then_inc(lin_mm, 1)
                pe.wait_ge(copied, past(3 * q + 1))
                linear(DIR, lin0, 0)
                slab_mm(q, 6, actor)
                pe.wait_ge(merged, past(4 * q + 1))
                pe.wait_ge(copied, past(3 * q + 2))
                linear(GEN, lin1, 1)
                with pe.Fori(7, SLABS) as s:
                    slab_mm(q, s, actor)
                pe.wait_ge(merged, past(4 * q + 2))
                pe.wait_ge(copied, past(3 * q + 3))
                linear(ACTR, lin0, 0)
            pe.wait_ge(or_step, 3)
            pe.wait_ge(merged, past(4 * NQ))
            nc.tensor.matmul(lin1[0:1, 0:1], worst[:, :], ones_f[:, :], start=True, stop=True).then_inc(verdict_mm, 1)

            def wide_mm(bank_sl, weights, entries, start=False):
                return nc.tensor.matmul(bank_sl[:, :], weights.rearrange("p o e -> p (o e)"), entries,
                                        start=start, stop=False, skip_group_check=True)

            def wide_half(q, s, h, chunks, bank_sl):
                for j in chunks:
                    last = wide_mm(bank_sl, wide_w[:, h, j, :, :], wide_x[:, h, j * COLS:(j + 1) * COLS])
                return last

            def wide_wait(q, s, h):
                pe.wait_ge(wide_conv[h], q * SLABS + s + 1)
                pe.wait_ge(wide_staged, (q * SLABS + s) * 4 + 2 * h + 2)

            def wide_slab(q, s, bank_sl):
                for h in range(2):
                    wide_wait(q, s, h)
                    wide_half(q, s, h, range(HALF), bank_sl).then_inc(wide_used[h], 1)

            pe.wait_ge(verdict, 1)
            with pe.If(pe.value_load(wide[0:1, 0:1], min_val=0, max_val=1) == 1):
                pe.wait_ge(wide_fixed, 2)
                with pe.Fori(0, NQ) as q:
                    pe.wait_ge(wide_tail_conv, q + 1)
                    wide_mm(dir_sl, wide_w_fixed[0:DIR_TAIL, W_DIRTAIL], wide_tail, True)
                    with pe.Fori(0, 2) as s:
                        wide_slab(q, s, dir_sl)
                    wide_wait(q, 2, 0)
                    wide_half(q, 2, 0, [0], dir_sl)
                    wide_mm(gen_sl, wide_w_fixed[:, W_GENRE], wide_x[:, 0, COLS:2 * COLS], True)
                    wide_mm(act_sl, wide_w[:, 0, 1], wide_x[:, 0, COLS:2 * COLS], True)
                    wide_half(q, 2, 0, range(2, HALF), act_sl).then_inc(wide_used[0], 1)
                    wide_wait(q, 2, 1)
                    wide_half(q, 2, 1, range(HALF), act_sl).then_inc(wide_used[1], 1)
                    with pe.Fori(3, SLABS) as s:
                        wide_slab(q, s, act_sl)
                    for n, (g, products_g, bank_lin) in enumerate(((DIR, slo[:, 0], dir_hm), (GEN, slo[:, 1], gen_hm),
                                                                   (ACTR, him[:, 0], act_hm))):
                        pe.wait_ge(wide_copied, 3 * q + n + 1)
                        for t in range(TILES):
                            last = nc.tensor.matmul(bank_lin[:, t * (E + 1):(t + 1) * (E + 1)], products_g[:, t * P:(t + 1) * P],
                                                    lin_low[:, g, :], start=True, stop=True)
                        last.then_inc(wide_lin, 1)


def _layout(a, np):
    x = np.zeros((CHUNKS * P, BATCH), a["r_actors_idx"].dtype)
    full_d, full_a = DIR_CHUNKS * P, ACT_CHUNKS * P
    x[0:full_d] = a["r_director_idx"][:, 0:full_d].T
    x[full_d:full_d + ACT_TAIL] = a["r_actors_idx"][:, full_a:].T
    x[full_d + GENRE_AT:full_d + GENRE_AT + GENRES] = a["r_genre_idx"].T
    x[full_d + P:] = a["r_actors_idx"][:, 0:full_a].T
    x = x.reshape(SLABS, 2, HALF, P, NQ, COLS).transpose(4, 0, 1, 3, 2, 5)
    stream = np.ascontiguousarray(x).reshape(NQ * SLABS, 2, P, HALF * COLS)
    w = np.zeros((WSLOTS, P, E), a["L0_rec_W_actor"].dtype)
    w[W_GENRE, GENRE_AT:GENRE_AT + GENRES] = a["L0_rec_W_genre"].T
    w[W_DIRTAIL, 0:DIR_TAIL] = a["L0_rec_W_director"][:, full_d:].T
    w[W_STREAM:W_STREAM + DIR_CHUNKS] = a["L0_rec_W_director"][:, 0:full_d].T.reshape(DIR_CHUNKS, P, E)
    w[W_STREAM + SHARED, 0:ACT_TAIL] = a["L0_rec_W_actor"][:, full_a:].T
    w[W_STREAM + SHARED + 1:] = a["L0_rec_W_actor"][:, 0:full_a].T.reshape(ACT_CHUNKS, P, E)
    return {
        "x_stream": stream,
        "x_dirtail": np.ascontiguousarray(a["r_director_idx"][:, full_d:].T),
        "rate": a["r_rate_idx"].reshape(1, BATCH),
        "w_all": np.ascontiguousarray(w.transpose(1, 0, 2)).reshape(P, WSLOTS * E),
        "emb_rate_t": np.ascontiguousarray(a["L0_rec_emb_rate"].T),
        "w_lin_t": np.ascontiguousarray(a["L0_rec_W_lin"].T),
        "bias": a["L0_rec_b_lin"].reshape(1, E),
    }


def kernel(**inputs):
    import numpy as np
    import concourse.bacc as bacc
    from concourse.bass_utils import run_bass_kernel_spmd

    laid = _layout({k: np.asarray(v) for k, v in inputs.items()}, np)
    nc = bacc.Bacc("TRN2", target_bir_lowering=False, num_devices=1)
    args = {k: nc.dram_tensor(k, v.shape, mybir.dt.from_np(v.dtype), kind="ExternalInput").ap() for k, v in laid.items()}
    out = nc.dram_tensor("out", (BATCH, E), F32, kind="ExternalOutput").ap()
    rec_head(nc, out=out, **args)
    result = run_bass_kernel_spmd(nc, [laid], core_ids=[0])
    return result.results[0]["out"]
```

```python
from contextlib import ExitStack

import concourse.bass as bass
from concourse import mybir

ALU = mybir.AluOpType
ACT = mybir.ActivationFunctionType
AX_X = mybir.AxisListType.X
BF16 = mybir.dt.bfloat16
F32 = mybir.dt.float32
I32 = mybir.dt.int32
U16 = mybir.dt.uint16
U32 = mybir.dt.uint32

P = 128
E = 64
RATES, GENRES, DIRECTORS, ACTORS = 6, 25, 2186, 8030
BATCH = 2048
NQ = 4
COLS = BATCH // NQ
TILES = COLS // P

DIR_CHUNKS = DIRECTORS // P
DIR_TAIL = DIRECTORS - DIR_CHUNKS * P
ACT_CHUNKS = ACTORS // P
ACT_TAIL = ACTORS - ACT_CHUNKS * P
GENRE_AT = 96
CHUNKS = DIR_CHUNKS + 1 + ACT_CHUNKS
SLAB = 8
HALF = SLAB // 2
SLABS = CHUNKS // SLAB
SHARED = DIR_CHUNKS
assert CHUNKS % SLAB == 0 and ACT_TAIL <= GENRE_AT and GENRE_AT + GENRES <= P and DIR_CHUNKS == 2 * SLAB + 1

W_GENRE, W_DIRTAIL, W_STREAM = 0, 1, 2
WSLOTS = W_STREAM + CHUNKS
W_FIRST = W_STREAM + DIR_CHUNKS
PIECE = 16
W_PIECES = [(0, 10), (10, W_FIRST)] + [(at, min(at + PIECE, WSLOTS)) for at in range(W_FIRST, WSLOTS, PIECE)]
XRING = 5
BRING = 2
assert SLABS % XRING == 0 and SLABS % BRING == 0
WORDS = HALF * COLS // 2
PARTS = [(0, 0, HALF), (1, 0, HALF - 2), (1, HALF - 2, HALF)]
SMALL_COLS = 3 * E + 3 * (E + 1) + 2 * E + RATES
ONE_BITS = 0x3F80
GEN, DIR, ACTR = 0, 1, 2


def rec_head(nc, x_stream, x_dirtail, rate, w_all, small, out):
    with ExitStack() as ctx:
        def sb(name, shape, dt):
            return ctx.enter_context(nc.sbuf_tensor(name, shape, dt))

        def bank(name):
            return ctx.enter_context(nc.psum_tensor(name, [P, COLS], F32))

        def sem(name):
            return ctx.enter_context(nc.semaphore(name))

        x_raw = sb("x_raw", [P, XRING, 2, HALF * COLS], I32)
        x_bf = sb("x_bf", [P, BRING, 2, HALF * COLS], BF16)
        w32 = sb("w32", [P, WSLOTS, E], F32)
        w_parts = sb("w_parts", [P, WSLOTS, 4, E], BF16)
        tail_raw = sb("tail_raw", [DIR_TAIL, COLS], I32)
        tail_bf = sb("tail_bf", [DIR_TAIL, COLS], BF16)
        rate_i = sb("rate_i", [RATES, COLS], I32)
        onehot = sb("onehot", [RATES + 1, COLS], F32)
        rate_wrap = sb("rate_wrap", [RATES, COLS], F32)
        row_no_i = sb("row_no_i", [RATES, 1], I32)
        row_no = sb("row_no", [RATES, 1], F32)
        small_sb = sb("small_sb", [P, SMALL_COLS], F32)
        at = 3 * E
        lin_twice = small_sb[:, 0:at].rearrange("p (g e) -> p g e", g=3)
        lin_low = small_sb[:, at:at + 3 * (E + 1)].rearrange("p (g e) -> p g e", g=3)
        at += 3 * (E + 1)
        lin_rate = small_sb[0:E, at:at + E]
        rate_table = small_sb[0:RATES + 1, at + E:at + 2 * E]
        emb_t = small_sb[0:E, at + 2 * E:at + 2 * E + RATES]
        products = sb("products", [P, 2, 2, COLS], F32)
        him = products[:, 0]
        slo = products[:, 1]
        w_rest = products[:, :, :, :].rearrange("p a b n -> p a (b n)").rearrange("p a (s e) -> p a s e", e=E)
        inv = sb("inv", [P, TILES, 1], F32)
        term = sb("term", [P, TILES, E], F32)
        rate_terms = sb("rate_terms", [P, NQ, TILES, E], F32)
        out_sb = sb("out_sb", [P, TILES, E], F32)
        seen = sb("seen", [P, 2, WORDS], U32)
        worst = sb("worst", [P, 1], F32)
        wide_x = x_raw[:, 0, :, :].bitcast(F32)
        wide_tail = tail_raw[:, :].bitcast(F32)
        wide_w = x_raw[:, 1, :, :].bitcast(F32).rearrange("p h (s o e) -> p h s o e", o=2, e=E)
        wide_w_fixed = x_raw[:, 2, 0, 0:2 * 2 * E].bitcast(F32).rearrange("p (s o e) -> p s o e", o=2, e=E)
        ones_f = sb("ones_f", [P, 1], F32)
        minus_one = sb("minus_one", [P, 1], F32)
        wide = sb("wide", [1, 1], I32)

        dir_hm, dir_sl = bank("dir_hm"), bank("dir_sl")
        gen_hm, gen_sl = bank("gen_hm"), bank("gen_sl")
        act_hm, act_sl = bank("act_hm"), bank("act_sl")
        lin0, lin1 = bank("lin0"), bank("lin1")

        landed = [[sem(f"x_landed_{r}_{part}") for part in range(len(PARTS))] for r in range(XRING)]
        w_landed = [sem(f"w_landed_{i}") for i in range(2)]
        tail_landed, rate_landed, small_landed = sem("tail_landed"), sem("rate_landed"), sem("small_landed")
        part0_conv, part1_conv = sem("part0_converted"), sem("part1_converted")
        part2_conv = [sem("part2_by_vector"), sem("part2_by_scalar")]
        converted = [[part0_conv], [part1_conv], part2_conv]
        checked = sem("checked")
        used = sem("slabs_used")
        hi_done, rest_done, mid_done, lo_done = sem("hi_done"), sem("rest_done"), sem("mid_done"), sem("lo_done")
        tail_conv, tail_seen = sem("tail_conv"), sem("tail_seen")
        zeroed = sem("zeroed")
        pool_step = sem("pool_step")
        rate_step = sem("rate_step")
        onehot_ready = sem("onehot_ready")
        table_mm, table_ready = sem("table_mm"), sem("table_ready")
        dir_mm, gen_mm = sem("dir_mm"), sem("gen_mm")
        copied = sem("products_copied")
        act_hm_copied = sem("act_hm_copied")
        inverted = sem("sums_inverted")
        lin_mm = sem("linear_mm")
        merged = sem("merged")
        term_ready = sem("term_ready")
        out_done, out_free = sem("out_done"), sem("out_free")
        half_checked, folded = sem("half_checked"), sem("folded")
        minus_one_set, excess = sem("minus_one_set"), sem("excess")
        verdict_mm, verdict = sem("verdict_mm"), sem("verdict")

        wide_landed = [sem(f"wide_landed_{h}") for h in range(2)]
        wide_conv = [sem(f"wide_converted_{h}") for h in range(2)]
        wide_used = [sem(f"wide_used_{h}") for h in range(2)]
        wide_tail_landed, wide_tail_conv = sem("wide_tail_landed"), sem("wide_tail_converted")
        wide_fixed, wide_staged = sem("wide_fixed"), sem("wide_staged")
        wide_copied, wide_lin = sem("wide_copied"), sem("wide_linear_mm")
        wide_step, wide_merged, wide_stored = sem("wide_step"), sem("wide_merged"), sem("wide_stored")
        wide_free = sem("wide_out_free")

        started = {"pe": [used, dir_mm, lin_mm, *wide_used], "act": [copied], "dve": [checked, half_checked, folded, tail_seen, merged], "pool": [out_free, wide_free]}

        def past(n):
            return n + 1

        block = ctx.enter_context(nc.Block())
        first_cols = W_FIRST * E

        @block.sync
        def _(sp):
            sp.dma_start(w32[:, 0:W_FIRST, :].rearrange("p s e -> p (s e)"), w_all[:, 0:first_cols]).then_inc(w_landed[0], 16)
            sp.dma_start(tail_raw[:, :], x_dirtail[:, 0:COLS]).then_inc(tail_landed, 16)
            sp.dma_start(rate_i[:, :], rate[:, 0:COLS].broadcast_to([RATES, COLS])).then_inc(rate_landed, 16)
            sp.dma_start(small_sb[:, :], small).then_inc(small_landed, 16)
            sp.dma_start(w32[:, W_FIRST:, :].rearrange("p s e -> p (s e)"), w_all[:, first_cols:]).then_inc(w_landed[1], 16)
            for r in range(XRING):
                for part, (h, lo, hi) in enumerate(PARTS):
                    sp.dma_start(x_raw[:, r, h, lo * COLS:hi * COLS], x_stream[r, h, :, lo * COLS:hi * COLS]
                                 ).then_inc(landed[r][part], 16)

            def refill(q, s):
                for part, (h, lo, hi) in enumerate(PARTS):
                    for signal in converted[part]:
                        sp.wait_ge(signal, q * SLABS + s + 1)
                    sp.dma_start(x_raw[:, s % XRING, h, lo * COLS:hi * COLS],
                                 x_stream[bass.ds(q * SLABS + s + XRING, 1), h, :, lo * COLS:hi * COLS
                                          ].rearrange("s p n -> (s p) n")).then_inc(landed[s % XRING][part], 16)

            def store(q):
                sp.wait_ge(merged, past(4 * q + 4))
                sp.dma_start(out[bass.ds(q * COLS, COLS), :].rearrange("(p t) e -> p t e", p=P), out_sb[:, :, :]
                             ).then_inc(out_done, 16)

            with sp.Fori(0, NQ - 1) as q:
                for s in range(SLABS):
                    if s == 4:
                        sp.wait_ge(tail_conv, q + 1)
                        sp.dma_start(tail_raw[:, :], x_dirtail[:, bass.ds((q + 1) * COLS, COLS)]).then_inc(tail_landed, 16)
                        sp.wait_ge(onehot_ready, q + 1)
                        sp.dma_start(rate_i[:, :], rate[:, bass.ds((q + 1) * COLS, COLS)].broadcast_to([RATES, COLS])
                                     ).then_inc(rate_landed, 16)
                    refill(q, s)
                store(q)
            for s in range(SLABS - XRING):
                refill(NQ - 1, s)
            store(NQ - 1)
            sp.wait_ge(verdict, 1)
            is_wide = sp.value_load(wide[0:1, 0:1], min_val=0, max_val=1)
            sp.wait_ge(out_done, 16 * NQ)
            with sp.If(is_wide == 1):
                with sp.Fori(0, NQ) as q:
                    sp.dma_start(tail_raw[:, :], x_dirtail[:, bass.ds(q * COLS, COLS)]).then_inc(wide_tail_landed, 16)
                    with sp.Fori(0, SLABS) as s:
                        slab = sp.snap(q * SLABS + s)
                        for h in range(2):
                            sp.wait_ge(wide_used[h], past(slab))
                            sp.dma_start(x_raw[:, 0, h, :], x_stream[bass.ds(slab, 1), h].rearrange("s p n -> (s p) n")
                                         ).then_inc(wide_landed[h], 16)
                    row = sp.snap(q * COLS)
                    sp.wait_ge(wide_merged, 3 * q + 3)
                    sp.dma_start(out[bass.ds(row, COLS), :].rearrange("(p t) e -> p t e", p=P), out_sb[:, :, :]
                                 ).then_inc(wide_stored, 16)
                    sp.wait_ge(wide_stored, 16 * q + 16)
                    sp.sem_inc(wide_free, 1)

        @block.gpsimd
        def _(pool):
            for signal in started["pool"]:
                pool.sem_inc(signal, 1)
            nc.gpsimd.memset(w_parts[:, :, 2, :], 1.0).then_inc(pool_step, 1)
            pool.wait_ge(pool_step, 1)
            nc.gpsimd.memset(w_parts[GENRE_AT:P, W_STREAM + SHARED, 2, :], 0.0).then_inc(pool_step, 1)
            pool.wait_ge(pool_step, 2)
            for start in range(0, GENRE_AT, 32):
                nc.gpsimd.memset(w_parts[start:start + 32, W_GENRE, 2, :], 0.0).then_inc(pool_step, 1)
                pool.wait_ge(pool_step, 3 + start // 32)
            nc.gpsimd.memset(ones_f[:, :], 1.0).then_inc(pool_step, 1)
            pool.wait_ge(pool_step, 6)
            nc.gpsimd.memset(onehot[:, :], 1.0).then_inc(pool_step, 1)
            pool.wait_ge(pool_step, 7)
            nc.gpsimd.iota(row_no_i[:, :], [[0, 1]], base=0, channel_multiplier=1).then_inc(pool_step, 1)
            pool.wait_ge(pool_step, 8)
            nc.gpsimd.tensor_copy(row_no[:, :], row_no_i[:, :]).then_inc(pool_step, 1)
            pool.wait_ge(pool_step, 9)
            for q in range(NQ):
                pool.wait_ge(rate_landed, 16 * q + 16)
                if q >= 1:
                    pool.wait_ge(lin_mm, past(4 * q))
                nc.gpsimd.tensor_copy(onehot[0:RATES, :], rate_i[:, :]).then_inc(rate_step, 1)
                pool.wait_ge(rate_step, 4 * q + 1)
                nc.gpsimd.tensor_scalar(rate_wrap[:, :], onehot[0:RATES, :], 0.0, float(RATES), ALU.is_lt, ALU.mult).then_inc(rate_step, 1)
                pool.wait_ge(rate_step, 4 * q + 2)
                nc.gpsimd.tensor_tensor(onehot[0:RATES, :], onehot[0:RATES, :], rate_wrap[:, :], ALU.add).then_inc(rate_step, 1)
                pool.wait_ge(rate_step, 4 * q + 3)
                nc.gpsimd.tensor_scalar(rate_wrap[:, :], onehot[0:RATES, :], 0.0, float(RATES - 1), ALU.max, ALU.min).then_inc(rate_step, 1)
                pool.wait_ge(rate_step, 4 * q + 4)
                nc.gpsimd.tensor_scalar(onehot[0:RATES, :], rate_wrap[:, :], row_no[:, 0:1], None, ALU.is_equal).then_inc(onehot_ready, 1)
                if q >= 1:
                    pool.wait_ge(out_done, 16 * q)
                    pool.sem_inc(out_free, 1)

        def group_copy(bank_hm, bank_sl, slot):
            nc.scalar.copy(slo[:, slot, :], bank_sl[:, :])
            nc.scalar.copy(him[:, slot, :], bank_hm[:, :]).then_inc(copied, 1)

        @block.scalar
        def _(act):
            for signal in started["act"]:
                act.sem_inc(signal, 1)
            def piece_mid(i):
                lo, hi = W_PIECES[i]
                act.wait_ge(rest_done, i + 1)
                nc.scalar.copy(w_parts[:, lo:hi, 1, :], w_rest[:, i % 2, 0:hi - lo, :]).then_inc(mid_done, 1)

            for i, (lo, hi) in enumerate(W_PIECES):
                act.wait_ge(w_landed[int(lo >= W_FIRST)], 16)
                nc.scalar.copy(w_parts[:, lo:hi, 0, :], w32[:, lo:hi, :]).then_inc(hi_done, 1)
                if i >= 1:
                    piece_mid(i - 1)
            piece_mid(len(W_PIECES) - 1)

            with act.Fori(0, NQ) as q:
                act.wait_ge(tail_landed, 16 * q + 16)
                act.wait_ge(dir_mm, past(q))
                act.wait_ge(tail_seen, past(q))
                nc.scalar.copy(tail_bf[:, :], tail_raw[:, :]).then_inc(tail_conv, 1)
                for s in range(SLABS):
                    act.wait_ge(landed[s % XRING][1], (q * (SLABS // XRING) + s // XRING + 1) * 16)
                    if s >= BRING:
                        act.wait_ge(used, past(q * SLABS + s - BRING + 1))
                        act.wait_ge(checked, past(q * SLABS + s - BRING + 1))
                    else:
                        act.wait_ge(used, past(q * SLABS))
                        act.wait_ge(checked, past(q * SLABS))
                    nc.scalar.copy(x_bf[:, s % BRING, 1, 0:(HALF - 2) * COLS], x_raw[:, s % XRING, 1, 0:(HALF - 2) * COLS]
                                   ).then_inc(part1_conv, 1)
                    act.wait_ge(landed[s % XRING][2], (q * (SLABS // XRING) + s // XRING + 1) * 16)
                    nc.scalar.copy(x_bf[:, s % BRING, 1, (HALF - 1) * COLS:], x_raw[:, s % XRING, 1, (HALF - 1) * COLS:]
                                   ).then_inc(part2_conv[1], 1)
                    if s == 4:
                        act.wait_ge(dir_mm, past(q + 1))
                        act.wait_ge(lin_mm, past(4 * q))
                        group_copy(dir_hm, dir_sl, 0)
                        act.wait_ge(gen_mm, q + 1)
                        group_copy(gen_hm, gen_sl, 1)
                act.wait_ge(used, past((q + 1) * SLABS))
                act.wait_ge(lin_mm, past(4 * q + 2))
                nc.scalar.copy(slo[:, 0, :], act_sl[:, :]).then_inc(copied, 1)

            act.wait_ge(minus_one_set, 1)
            act.wait_ge(folded, past(NQ))
            nc.scalar.activation(x_bf[:, 0, 0, :], seen[:, 0, :].bitcast(U16), ACT.Relu, bias=minus_one[:, 0:1],
                                 accum_out=worst[:, :]).then_inc(excess, 1)

            act.wait_ge(verdict, 1)
            with act.If(act.value_load(wide[0:1, 0:1], min_val=0, max_val=1) == 1):
                with act.Fori(0, NQ) as q:
                    act.wait_ge(wide_used[1], past(q * SLABS + SLABS))
                    nc.scalar.copy(slo[:, 0, :], dir_sl[:, :]).then_inc(wide_copied, 1)
                    nc.scalar.copy(slo[:, 1, :], gen_sl[:, :]).then_inc(wide_copied, 1)
                    nc.scalar.copy(him[:, 0, :], act_sl[:, :]).then_inc(wide_copied, 1)

        @block.vector
        def _(dve):
            for signal in started["dve"]:
                dve.sem_inc(signal, 1)
            nc.vector.memset(seen[:, :, :], 0).then_inc(zeroed, 1)
            nc.vector.memset(minus_one[:, :], -float(ONE_BITS)).then_inc(minus_one_set, 1)

            def piece_lo(i):
                lo, hi = W_PIECES[i]
                dve.wait_ge(mid_done, i + 1)
                nc.vector.tensor_tensor(w_parts[:, lo:hi, 3, :], w_rest[:, i % 2, 0:hi - lo, :], w_parts[:, lo:hi, 1, :],
                                        ALU.subtract).then_inc(lo_done, 1)

            for i, (lo, hi) in enumerate(W_PIECES):
                dve.wait_ge(hi_done, i + 1)
                if i >= 2:
                    dve.wait_ge(lo_done, i - 1)
                nc.vector.tensor_tensor(w_rest[:, i % 2, 0:hi - lo, :], w32[:, lo:hi, :], w_parts[:, lo:hi, 0, :],
                                        ALU.subtract).then_inc(rest_done, 1)
                if i >= 1:
                    piece_lo(i - 1)
            piece_lo(len(W_PIECES) - 1)
            dve.wait_ge(zeroed, 1)
            dve.wait_ge(table_mm, 1)
            nc.vector.tensor_copy(rate_table[0:RATES], lin0[0:RATES, 0:E]).then_inc(table_ready, 1)

            def add_term(q, order, bank_lin):
                so_far = out_sb[:, :, :] if order > 1 else rate_terms[:, bass.ds(q, 1)].rearrange("p q t e -> p (q t) e")
                lin = bank_lin[:, 0:TILES * (E + 1)].rearrange("p (t e) -> p t e", t=TILES)
                dve.wait_ge(lin_mm, past(4 * q + order + 1))
                nc.vector.reciprocal(inv[:, :, :], lin[:, :, E:E + 1]).then_inc(inverted, 1)
                dve.wait_ge(inverted, 3 * q + order)
                nc.vector.tensor_tensor(term[:, :, :], lin[:, :, 0:E], inv[:, :, :].broadcast_to([P, TILES, E]),
                                        ALU.mult).then_inc(term_ready, 1)
                dve.wait_ge(term_ready, 3 * q + order)
                dve.wait_ge(merged, past(4 * q + order))
                nc.vector.tensor_tensor(out_sb[:, :, :], so_far, term[:, :, :], ALU.add).then_inc(merged, 1)

            with dve.Fori(0, NQ) as q:
                dve.wait_ge(tail_conv, q + 1)
                dve.wait_ge(folded, past(q))
                seen_tail = seen[0:DIR_TAIL, 0, 0:COLS // 2]
                nc.vector.tensor_tensor(seen_tail, seen_tail, tail_bf[:, :].bitcast(U32), ALU.bitwise_or).then_inc(tail_seen, 1)
                dve.wait_ge(tail_seen, past(q + 1))
                for s in range(SLABS):
                    dve.wait_ge(landed[s % XRING][0], (q * (SLABS // XRING) + s // XRING + 1) * 16)
                    if s >= BRING:
                        dve.wait_ge(used, past(q * SLABS + s - BRING + 1))
                    else:
                        dve.wait_ge(used, past(q * SLABS))
                    nc.vector.tensor_copy(x_bf[:, s % BRING, 0, :], x_raw[:, s % XRING, 0, :]).then_inc(part0_conv, 1)
                    dve.wait_ge(part0_conv, q * SLABS + s + 1)
                    dve.wait_ge(half_checked, past(q * SLABS + s))
                    nc.vector.tensor_tensor(seen[:, 0, :], seen[:, 0, :], x_bf[:, s % BRING, 0, :].bitcast(U32),
                                            ALU.bitwise_or).then_inc(half_checked, 1)
                    dve.wait_ge(landed[s % XRING][2], (q * (SLABS // XRING) + s // XRING + 1) * 16)
                    nc.vector.tensor_copy(x_bf[:, s % BRING, 1, (HALF - 2) * COLS:(HALF - 1) * COLS],
                                          x_raw[:, s % XRING, 1, (HALF - 2) * COLS:(HALF - 1) * COLS]
                                          ).then_inc(part2_conv[0], 1)
                    dve.wait_ge(part1_conv, q * SLABS + s + 1)
                    dve.wait_ge(part2_conv[0], q * SLABS + s + 1)
                    dve.wait_ge(part2_conv[1], q * SLABS + s + 1)
                    dve.wait_ge(checked, past(q * SLABS + s))
                    nc.vector.tensor_tensor(seen[:, 1, :], seen[:, 1, :], x_bf[:, s % BRING, 1, :].bitcast(U32),
                                            ALU.bitwise_or).then_inc(checked, 1)
                    if s == 6:
                        dve.wait_ge(lin_mm, past(4 * q + 1))
                        rate_term = lin1[:, 0:TILES * (E + 1)].rearrange("p (t e) -> p t e", t=TILES)[:, :, 0:E]
                        nc.vector.tensor_copy(rate_terms[:, bass.ds(q, 1)].rearrange("p q t e -> p (q t) e"), rate_term
                                              ).then_inc(merged, 1)
                        dve.wait_ge(out_free, past(q))
                        add_term(q, 1, lin0)
                    if s == 7:
                        add_term(q, 2, lin1)
                dve.wait_ge(used, past((q + 1) * SLABS))
                dve.wait_ge(lin_mm, past(4 * q + 2))
                nc.vector.tensor_copy(him[:, 0, :], act_hm[:, :]).then_inc(act_hm_copied, 1)
                dve.wait_ge(half_checked, past((q + 1) * SLABS))
                dve.wait_ge(checked, past((q + 1) * SLABS))
                nc.vector.tensor_tensor(seen[:, 0, :], seen[:, 0, :], seen[:, 1, :], ALU.bitwise_or).then_inc(folded, 1)
                add_term(q, 3, lin0)

            dve.wait_ge(verdict_mm, 1)
            nc.vector.tensor_scalar(wide[:, :], lin1[0:1, 0:1], 0.0, None, ALU.is_gt).then_inc(verdict, 1)

            dve.wait_ge(verdict, 1)
            with dve.If(dve.value_load(wide[0:1, 0:1], min_val=0, max_val=1) == 1):
                nc.vector.tensor_copy(wide_w_fixed[:, :, 0, :], w_parts[:, 0:2, 2, :]).then_inc(wide_fixed, 1)
                nc.vector.tensor_copy(wide_w_fixed[:, :, 1, :], w32[:, 0:2, :]).then_inc(wide_fixed, 1)
                with dve.Fori(0, NQ) as q:
                    dve.wait_ge(wide_tail_landed, 16 * q + 16)
                    nc.vector.tensor_copy(wide_tail, tail_raw[:, :]).then_inc(wide_tail_conv, 1)
                    with dve.Fori(0, SLABS) as s:
                        for h in range(2):
                            slots = bass.ds(s * SLAB + h * HALF + W_STREAM, HALF)
                            dve.wait_ge(wide_landed[h], (q * SLABS + s) * 16 + 16)
                            nc.vector.tensor_copy(wide_w[:, h, 0:HALF, 0, :], w_parts[:, slots, 2, :]).then_inc(wide_staged, 1)
                            nc.vector.tensor_copy(wide_w[:, h, 0:HALF, 1, :], w32[:, slots, :]).then_inc(wide_staged, 1)
                            nc.vector.tensor_copy(wide_x[:, h, :], x_raw[:, 0, h, :]).then_inc(wide_conv[h], 1)
                    dve.wait_ge(wide_free, past(q))
                    for g, bank_lin in enumerate((dir_hm, gen_hm, act_hm)):
                        lin = bank_lin[:, 0:TILES * (E + 1)].rearrange("p (t e) -> p t e", t=TILES)
                        so_far = out_sb[:, :, :] if g else rate_terms[:, bass.ds(q, 1)].rearrange("p q t e -> p (q t) e")
                        dve.wait_ge(wide_lin, 3 * q + g + 1)
                        nc.vector.reciprocal(inv[:, :, :], lin[:, :, E:E + 1]).then_inc(wide_step, 1)
                        dve.wait_ge(wide_step, 6 * q + 2 * g + 1)
                        nc.vector.tensor_tensor(term[:, :, :], lin[:, :, 0:E], inv[:, :, :].broadcast_to([P, TILES, E]),
                                                ALU.mult).then_inc(wide_step, 1)
                        dve.wait_ge(wide_step, 6 * q + 2 * g + 2)
                        nc.vector.tensor_tensor(out_sb[:, :, :], so_far, term[:, :, :], ALU.add).then_inc(wide_merged, 1)
                        dve.wait_ge(wide_merged, 3 * q + g + 1)

        @block.tensor
        def _(pe):
            for signal in started["pe"]:
                pe.sem_inc(signal, 1)
            def group_mm(slot, rhs, bank_hm, bank_sl, start, rows=P):
                nc.tensor.matmul(bank_hm[:, :], w_parts[0:rows, slot, 0:2, :].rearrange("p a e -> p (a e)"), rhs,
                                 start=start, stop=False, skip_group_check=True)
                return nc.tensor.matmul(bank_sl[:, :], w_parts[0:rows, slot, 2:4, :].rearrange("p a e -> p (a e)"), rhs,
                                        start=start, stop=False, skip_group_check=True)

            def chunk(s, j):
                return x_bf[:, bass.ds(s % BRING, 1), j // HALF, (j % HALF) * COLS:(j % HALF + 1) * COLS].rearrange("p s n -> p (s n)")

            def slot_mm(s, j, banks, start=False):
                hm, sl = banks
                w_hm = w_parts[:, bass.ds(s * SLAB + j + W_STREAM, 1), 0:2, :].rearrange("p s a e -> p (s a e)")
                w_sl = w_parts[:, bass.ds(s * SLAB + j + W_STREAM, 1), 2:4, :].rearrange("p s a e -> p (s a e)")
                nc.tensor.matmul(hm[:, :], w_hm, chunk(s, j), start=start, stop=False, skip_group_check=True)
                return nc.tensor.matmul(sl[:, :], w_sl, chunk(s, j), start=start, stop=False, skip_group_check=True)

            def chunk_wait(q, s, j):
                if j == 0:
                    pe.wait_ge(part0_conv, q * SLABS + s + 1)
                if j == HALF:
                    pe.wait_ge(part1_conv, q * SLABS + s + 1)
                if j >= SLAB - 2:
                    pe.wait_ge(part2_conv[j - (SLAB - 2)], q * SLABS + s + 1)

            def slab_mm(q, s, banks):
                for j in range(SLAB):
                    chunk_wait(q, s, j)
                    last = slot_mm(s, j, banks)
                last.then_inc(used, 1)

            def linear(g, bank_lin, slot):
                for t in range(TILES):
                    at = t * (E + 1)
                    cols = slice(t * P, (t + 1) * P)
                    nc.tensor.matmul(bank_lin[:, at:at + E + 1], slo[:, slot, cols], lin_low[:, g, :],
                                     start=True, stop=False, skip_group_check=True)
                    last = nc.tensor.matmul(bank_lin[:, at:at + E], him[:, slot, cols], lin_twice[:, g, :],
                                            start=False, stop=True, skip_group_check=True)
                last.then_inc(lin_mm, 1)

            pe.wait_ge(small_landed, 16)
            nc.tensor.matmul(lin0[0:RATES, 0:E], emb_t, lin_rate, start=True, stop=True).then_inc(table_mm, 1)
            pe.wait_ge(pool_step, 5)
            pe.wait_ge(lo_done, len(W_PIECES))
            pe.wait_ge(mid_done, len(W_PIECES))
            pe.wait_ge(hi_done, len(W_PIECES))
            pe.wait_ge(table_ready, 1)
            director, actor, genre = (dir_hm, dir_sl), (act_hm, act_sl), (gen_hm, gen_sl)
            with pe.Fori(0, NQ) as q:
                pe.wait_ge(tail_conv, q + 1)
                group_mm(W_DIRTAIL, tail_bf[:, :], *director, True, DIR_TAIL)
                with pe.Fori(0, 2) as s:
                    slab_mm(q, s, director)
                chunk_wait(q, 2, 0)
                slot_mm(2, 0, director).then_inc(dir_mm, 1)
                group_mm(W_GENRE, chunk(2, 1), *genre, True).then_inc(gen_mm, 1)
                pe.wait_ge(copied, past(3 * q))
                slot_mm(2, 1, actor, True)
                for j in range(2, SLAB):
                    chunk_wait(q, 2, j)
                    last = slot_mm(2, j, actor)
                last.then_inc(used, 1)
                with pe.Fori(3, 6) as s:
                    slab_mm(q, s, actor)
                pe.wait_ge(merged, past(4 * q))
                pe.wait_ge(onehot_ready, q + 1)
                for t in range(TILES):
                    last = nc.tensor.matmul(lin1[:, t * (E + 1):t * (E + 1) + E], onehot[:, t * P:(t + 1) * P],
                                            rate_table, start=True, stop=True)
                last.then_inc(lin_mm, 1)
                pe.wait_ge(copied, past(3 * q + 1))
                linear(DIR, lin0, 0)
                slab_mm(q, 6, actor)
                pe.wait_ge(merged, past(4 * q + 1))
                pe.wait_ge(copied, past(3 * q + 2))
                linear(GEN, lin1, 1)
                with pe.Fori(7, SLABS) as s:
                    slab_mm(q, s, actor)
                pe.wait_ge(merged, past(4 * q + 2))
                pe.wait_ge(copied, past(3 * q + 3))
                pe.wait_ge(act_hm_copied, q + 1)
                linear(ACTR, lin0, 0)
            pe.wait_ge(excess, 1)
            pe.wait_ge(merged, past(4 * NQ))
            nc.tensor.matmul(lin1[0:1, 0:1], worst[:, :], ones_f[:, :], start=True, stop=True).then_inc(verdict_mm, 1)

            def wide_mm(bank_sl, weights, entries, start=False):
                return nc.tensor.matmul(bank_sl[:, :], weights.rearrange("p o e -> p (o e)"), entries,
                                        start=start, stop=False, skip_group_check=True)

            def wide_half(h, chunks, bank_sl):
                for j in chunks:
                    last = wide_mm(bank_sl, wide_w[:, h, j, :, :], wide_x[:, h, j * COLS:(j + 1) * COLS])
                return last

            def wide_wait(q, s, h):
                pe.wait_ge(wide_conv[h], q * SLABS + s + 1)
                pe.wait_ge(wide_staged, (q * SLABS + s) * 4 + 2 * h + 2)

            def wide_slab(q, s, bank_sl):
                for h in range(2):
                    wide_wait(q, s, h)
                    wide_half(h, range(HALF), bank_sl).then_inc(wide_used[h], 1)

            pe.wait_ge(verdict, 1)
            with pe.If(pe.value_load(wide[0:1, 0:1], min_val=0, max_val=1) == 1):
                pe.wait_ge(wide_fixed, 2)
                with pe.Fori(0, NQ) as q:
                    pe.wait_ge(wide_tail_conv, q + 1)
                    wide_mm(dir_sl, wide_w_fixed[0:DIR_TAIL, W_DIRTAIL], wide_tail, True)
                    with pe.Fori(0, 2) as s:
                        wide_slab(q, s, dir_sl)
                    wide_wait(q, 2, 0)
                    wide_half(0, [0], dir_sl)
                    wide_mm(gen_sl, wide_w_fixed[:, W_GENRE], wide_x[:, 0, COLS:2 * COLS], True)
                    wide_mm(act_sl, wide_w[:, 0, 1], wide_x[:, 0, COLS:2 * COLS], True)
                    wide_half(0, range(2, HALF), act_sl).then_inc(wide_used[0], 1)
                    wide_wait(q, 2, 1)
                    wide_half(1, range(HALF), act_sl).then_inc(wide_used[1], 1)
                    with pe.Fori(3, SLABS) as s:
                        wide_slab(q, s, act_sl)
                    for n, (g, products_g, bank_lin) in enumerate(((DIR, slo[:, 0], dir_hm), (GEN, slo[:, 1], gen_hm),
                                                                   (ACTR, him[:, 0], act_hm))):
                        pe.wait_ge(wide_copied, 3 * q + n + 1)
                        for t in range(TILES):
                            last = nc.tensor.matmul(bank_lin[:, t * (E + 1):(t + 1) * (E + 1)], products_g[:, t * P:(t + 1) * P],
                                                    lin_low[:, g, :], start=True, stop=True)
                        last.then_inc(wide_lin, 1)


def _layout(a, np):
    def columns(x):
        return x.reshape(*x.shape[:-1], NQ, P, TILES).swapaxes(-1, -2).reshape(x.shape)

    x = np.zeros((CHUNKS * P, BATCH), a["r_actors_idx"].dtype)
    full_d, full_a = DIR_CHUNKS * P, ACT_CHUNKS * P
    x[0:full_d] = a["r_director_idx"][:, 0:full_d].T
    x[full_d:full_d + ACT_TAIL] = a["r_actors_idx"][:, full_a:].T
    x[full_d + GENRE_AT:full_d + GENRE_AT + GENRES] = a["r_genre_idx"].T
    x[full_d + P:] = a["r_actors_idx"][:, 0:full_a].T
    x = columns(x).reshape(SLABS, 2, HALF, P, NQ, COLS).transpose(4, 0, 1, 3, 2, 5)
    stream = np.ascontiguousarray(x).reshape(NQ * SLABS, 2, P, HALF * COLS)
    w = np.zeros((WSLOTS, P, E), a["L0_rec_W_actor"].dtype)
    w[W_GENRE, GENRE_AT:GENRE_AT + GENRES] = a["L0_rec_W_genre"].T
    w[W_DIRTAIL, 0:DIR_TAIL] = a["L0_rec_W_director"][:, full_d:].T
    w[W_STREAM:W_STREAM + DIR_CHUNKS] = a["L0_rec_W_director"][:, 0:full_d].T.reshape(DIR_CHUNKS, P, E)
    w[W_STREAM + SHARED, 0:ACT_TAIL] = a["L0_rec_W_actor"][:, full_a:].T
    w[W_STREAM + SHARED + 1:] = a["L0_rec_W_actor"][:, 0:full_a].T.reshape(ACT_CHUNKS, P, E)
    w_lin_t = a["L0_rec_W_lin"].T.reshape(4, E, E)
    small = np.zeros((P, SMALL_COLS), w.dtype)
    low = 3 * E
    rate_at = low + 3 * (E + 1)
    for g in range(3):
        small[0:E, g * E:(g + 1) * E] = w_lin_t[g + 1]
        small[E:P, g * E:(g + 1) * E] = w_lin_t[g + 1]
        small[E:P, low + g * (E + 1):low + g * (E + 1) + E] = w_lin_t[g + 1]
        small[0, low + g * (E + 1) + E] = 1.0
    small[0:E, rate_at:rate_at + E] = w_lin_t[0]
    small[RATES, rate_at + E:rate_at + 2 * E] = a["L0_rec_b_lin"]
    small[0:E, rate_at + 2 * E:] = a["L0_rec_emb_rate"].T
    return {
        "x_stream": stream,
        "x_dirtail": np.ascontiguousarray(columns(a["r_director_idx"][:, full_d:].T)),
        "rate": columns(a["r_rate_idx"].reshape(1, BATCH)),
        "w_all": np.ascontiguousarray(w.transpose(1, 0, 2)).reshape(P, WSLOTS * E),
        "small": small,
    }


def kernel(**inputs):
    import numpy as np
    import concourse.bacc as bacc
    from concourse.bass_utils import run_bass_kernel_spmd

    laid = _layout({k: np.asarray(v) for k, v in inputs.items()}, np)
    nc = bacc.Bacc("TRN2", target_bir_lowering=False, num_devices=1)
    args = {k: nc.dram_tensor(k, v.shape, mybir.dt.from_np(v.dtype), kind="ExternalInput").ap() for k, v in laid.items()}
    out = nc.dram_tensor("out", (BATCH, E), F32, kind="ExternalOutput").ap()
    rec_head(nc, out=out, **args)
    result = run_bass_kernel_spmd(nc, [laid], core_ids=[0])
    return result.results[0]["out"]
```
